# Optimizing a Trainium2 kernel written in Bass

```python
import numpy as np
import jax
import jax.numpy as jnp

def _softmax(x, axis=-1):
    return jax.nn.softmax(x, axis=axis)

def _gelu(x):
    return jax.nn.gelu(x, approximate=True)

def _silu(x):
    return jax.nn.silu(x)

def _sigmoid(x):
    return jax.nn.sigmoid(x)

def _layernorm(x, axis=-1, eps=1e-05):
    m = jnp.mean(x, axis=axis, keepdims=True)
    v = jnp.var(x, axis=axis, keepdims=True)
    return (x - m) / jnp.sqrt(v + eps)

def _scatter_add(tgt, idx, src, axis=0):
    return tgt.at[idx].add(src)

def _segment_sum(src, seg, n):
    return jax.ops.segment_sum(src, seg, n)
kernel_name = 'mk_xattn_ffn_d1_seqx_r4_0a0306'

def setup_inputs(seed: int=0):
    np.random.seed(seed)
    _w = jnp.asarray

    def _rec_inputs():
        import jax
        import jax.numpy as jnp
        _rk = jax.random.key(seed)
        x = -0.000929 + 1 * jax.random.normal(jax.random.fold_in(_rk, 1), (16, 512, 256), jnp.float32)
        _lenS = 512 - jax.random.randint(jax.random.fold_in(_rk, 7), (16,), 0, max(1, 512 // 4) + 1, jnp.int32)
        _lenS2 = 1601 - jax.random.randint(jax.random.fold_in(_rk, 8), (16,), 0, max(1, 1601 // 4) + 1, jnp.int32)
        _ctx_1024P = jax.random.normal(jax.random.fold_in(_rk, 11), (16, 16, 256), jnp.float32)
        _ctx_1024c = jax.random.dirichlet(jax.random.fold_in(_rk, 511), 0.3 * jnp.ones((16,), jnp.float32), (16, 1601))
        _ctx_1024t = jnp.einsum('bsk,bkd->bsd', _ctx_1024c, _ctx_1024P)
        _ctx_1024t = _ctx_1024t * jax.lax.rsqrt(jnp.mean(jnp.square(_ctx_1024t)) + 1e-12) * 0.953939
        ctx_1024 = 2.81802e-05 + 1.00001 * (_ctx_1024t + 0.3 * jax.random.normal(jax.random.fold_in(_rk, 611), (16, 1601, 256), jnp.float32))
        _validS = jnp.arange(512)[None, :] < _lenS[:, None]
        _validS2 = jnp.arange(1601)[None, :] < _lenS2[:, None]
        _causal = jnp.tril(jnp.ones((512, 512), dtype=bool))
        mask_BxS2_bf0 = jnp.logical_not(jnp.ones((16, 1601), dtype=bool))
        return (x, ctx_1024, mask_BxS2_bf0)
    x, ctx_1024, mask_BxS2_bf0 = _rec_inputs()

    def _L0_xattn_setup():
        import jax, jax.numpy as jnp
        import numpy as np
        D_MODEL = 256
        NUM_HEADS = 16
        STRIDE = 4
        HEAD_DIM = D_MODEL // NUM_HEADS
        SCALE = HEAD_DIM ** (-0.5)
        key = jax.random.key(seed)
        ks = jax.random.split(key, 12)
        B, T, S = (2, 128, 2048)
        inp = {'query': jax.random.normal(ks[0], (B, T, D_MODEL), jnp.float32), 'key': jax.random.normal(ks[1], (B, S, D_MODEL), jnp.float32), 'value': jax.random.normal(ks[2], (B, S, D_MODEL), jnp.float32), 'key_padding_mask': jnp.zeros((B, S), dtype=bool)}
        s = 1.0 / np.sqrt(D_MODEL)
        inp['Wq'] = jax.random.normal(ks[3], (D_MODEL, D_MODEL), jnp.float32) * s
        inp['bq'] = jnp.zeros((D_MODEL,), jnp.float32)
        inp['Wk'] = jax.random.normal(ks[4], (D_MODEL, D_MODEL), jnp.float32) * s
        inp['bk'] = jnp.zeros((D_MODEL,), jnp.float32)
        inp['Wv'] = jax.random.normal(ks[5], (D_MODEL, D_MODEL), jnp.float32) * s
        inp['bv'] = jnp.zeros((D_MODEL,), jnp.float32)
        inp['Wo'] = jax.random.normal(ks[6], (D_MODEL, D_MODEL), jnp.float32) * s
        inp['bo'] = jnpp = jnp.zeros((D_MODEL,), jnp.float32)
        return inp
    _L0_xattn_all = _L0_xattn_setup()
    _L0_xattn_in = {k: v for k, v in _L0_xattn_all.items() if k in ('Wq', 'bq', 'Wk', 'bk', 'Wv', 'bv', 'Wo', 'bo')}
    del _L0_xattn_all

    def _L0_ffn_setup():
        import jax, jax.numpy as jnp
        import numpy as np
        E = 8
        K = 2
        S = 1
        THRESHOLD = 0.7
        NORM_TOPK = True
        H = 256
        F = 256
        B, SEQ = (2, 256)
        key = jax.random.key(seed)
        k1, k2, k3, k4, k5 = jax.random.split(key, 5)
        hidden_states = jax.random.normal(k1, (B, SEQ, H), jnp.float32)
        gate_weight = jax.random.normal(k2, (E, H), jnp.float32) * 0.02
        gate_up_proj = jax.random.normal(k3, (E, 2 * F, H), jnp.float32) * 0.02
        down_proj = jax.random.normal(k4, (E, H, F), jnp.float32) * 0.02
        sim = jax.random.uniform(k5, (E, E), jnp.float32)
        sim = (sim + sim.T) / 2.0
        sim = sim.at[jnp.arange(E), jnp.arange(E)].set(1.0)
        return {'hidden_states': hidden_states, 'gate_weight': gate_weight, 'gate_up_proj': gate_up_proj, 'down_proj': down_proj, 'similarity_matrix': sim}
    _L0_ffn_all = _L0_ffn_setup()
    _L0_ffn_in = {k: v for k, v in _L0_ffn_all.items() if k in ('gate_weight', 'gate_up_proj', 'down_proj', 'similarity_matrix')}
    del _L0_ffn_all
    return {'x': x, 'ctx_1024': ctx_1024, 'mask_BxS2_bf0': mask_BxS2_bf0, 'L0_xattn_Wq': _L0_xattn_in['Wq'], 'L0_xattn_bq': _L0_xattn_in['bq'], 'L0_xattn_Wk': _L0_xattn_in['Wk'], 'L0_xattn_bk': _L0_xattn_in['bk'], 'L0_xattn_Wv': _L0_xattn_in['Wv'], 'L0_xattn_bv': _L0_xattn_in['bv'], 'L0_xattn_Wo': _L0_xattn_in['Wo'], 'L0_xattn_bo': _L0_xattn_in['bo'], 'L0_ffn_gate_weight': _L0_ffn_in['gate_weight'], 'L0_ffn_gate_up_proj': _L0_ffn_in['gate_up_proj'], 'L0_ffn_down_proj': _L0_ffn_in['down_proj'], 'L0_ffn_similarity_matrix': _L0_ffn_in['similarity_matrix']}

def reference(x, ctx_1024, mask_BxS2_bf0, L0_xattn_Wq, L0_xattn_bq, L0_xattn_Wk, L0_xattn_bk, L0_xattn_Wv, L0_xattn_bv, L0_xattn_Wo, L0_xattn_bo, L0_ffn_gate_weight, L0_ffn_gate_up_proj, L0_ffn_down_proj, L0_ffn_similarity_matrix):
    import jax
    import jax.numpy as jnp

    def _L0_xattn_ref(query, key, value, key_padding_mask, Wq, bq, Wk, bk, Wv, bv, Wo, bo):
        import jax, jax.numpy as jnp
        import numpy as np
        D_MODEL = 256
        NUM_HEADS = 16
        STRIDE = 4
        HEAD_DIM = D_MODEL // NUM_HEADS
        SCALE = HEAD_DIM ** (-0.5)
        B, T, _ = query.shape
        S = key.shape[1]
        q = (query @ Wq + bq).reshape(B, T, NUM_HEADS, HEAD_DIM).transpose(0, 2, 1, 3)
        k = (key @ Wk + bk).reshape(B, S, NUM_HEADS, HEAD_DIM).transpose(0, 2, 1, 3)
        v = (value @ Wv + bv).reshape(B, S, NUM_HEADS, HEAD_DIM).transpose(0, 2, 1, 3)
        scores = jnp.einsum('bhtd,bhsd->bhts', q, k) * SCALE
        s_idx = jnp.arange(S)[None, None, None, :]
        h_idx = jnp.arange(NUM_HEADS)[None, :, None, None]
        hepos_mask = (s_idx - h_idx) % STRIDE != 0
        scores = jnp.where(hepos_mask, -jnp.inf, scores)
        scores = jnp.where(key_padding_mask[:, None, None, :], -jnp.inf, scores)
        attn = jax.nn.softmax(scores, axis=-1)
        context = jnp.einsum('bhts,bhsd->bhtd', attn, v)
        context = context.transpose(0, 2, 1, 3).reshape(B, T, D_MODEL)
        return context @ Wo + bo

    def _L0_ffn_ref(hidden_states, gate_weight, gate_up_proj, down_proj, similarity_matrix):
        import jax, jax.numpy as jnp
        import numpy as np
        E = 8
        K = 2
        S = 1
        THRESHOLD = 0.7
        NORM_TOPK = True
        H = 256
        F = 256
        B, SEQ = (2, 256)
        b, s, h = hidden_states.shape
        x = hidden_states.reshape(-1, h)
        N = x.shape[0]
        logits = x @ gate_weight.T
        probs = jax.nn.softmax(logits.astype(jnp.float32), axis=-1)
        top_w, top_i = jax.lax.top_k(probs, K)
        if NORM_TOPK:
            top_w = top_w / jnp.clip(jnp.sum(top_w, -1, keepdims=True), 1e-12)
        primary_mask = jnp.zeros((E,), bool).at[top_i[:, :S].reshape(-1)].set(True)
        sim = jnp.where(primary_mask[None, :], similarity_matrix.astype(jnp.float32), -jnp.inf)
        best_j = jnp.argmax(sim, axis=-1)
        best_sim = jnp.max(sim, axis=-1)
        ids = jnp.arange(E)
        expert_map = jnp.where(~primary_mask & (best_sim >= THRESHOLD), best_j, ids)
        rerouted = expert_map[top_i]
        rows = jnp.arange(N)[:, None]
        dense = jnp.zeros((N, E), top_w.dtype).at[rows, rerouted].add(top_w)
        fw, fi = jax.lax.top_k(dense, K)
        combine = jnp.zeros((N, E), fw.dtype).at[rows, fi].add(jnp.where(fw > 0, fw, 0.0))
        gu = jnp.einsum('nh,efh->enf', x, gate_up_proj)
        g, u = jnp.split(gu, 2, axis=-1)
        hmid = jax.nn.silu(g) * u
        y = jnp.einsum('enf,ehf->enh', hmid, down_proj)
        out = jnp.einsum('ne,enh->nh', combine, y)
        return out.reshape(b, s, h)
    x = x + _L0_xattn_ref(_layernorm(x, axis=-1), ctx_1024, ctx_1024, mask_BxS2_bf0, L0_xattn_Wq, L0_xattn_bq, L0_xattn_Wk, L0_xattn_bk, L0_xattn_Wv, L0_xattn_bv, L0_xattn_Wo, L0_xattn_bo)
    x = x + _L0_ffn_ref(_layernorm(x, axis=-1), L0_ffn_gate_weight, L0_ffn_gate_up_proj, L0_ffn_down_proj, L0_ffn_similarity_matrix)
    return x

_drawn_inputs = setup_inputs


def setup_inputs(seed=0):
    import zlib

    import numpy as np

    out = dict(_drawn_inputs(seed))
    spreads = {'L0_xattn_bq': (0.0, 0.395),
     'L0_xattn_bk': (0.0, 0.8),
     'L0_xattn_bv': (0.0, 0.1),
     'L0_xattn_bo': (0.0, 0.1)}
    factors = {'L0_ffn_gate_weight': 6.164, 'L0_ffn_gate_up_proj': 5.376, 'L0_ffn_down_proj': 5.378}
    for name, (base, spread) in spreads.items():
        noise = np.random.default_rng([zlib.crc32(name.encode()), seed]).standard_normal(out[name].shape)
        drawn = base * np.exp(spread * noise) if base else spread * noise
        out[name] = jnp.asarray(drawn.astype(out[name].dtype))
    for name, factor in factors.items():
        out[name] = (out[name] * factor).astype(out[name].dtype)
    return out
```

```python
from contextlib import ExitStack

import concourse.bass as bass
from concourse import mybir

ALU = mybir.AluOpType
ACT = mybir.ActivationFunctionType
AX = mybir.AxisListType.X
F32 = mybir.dt.float32
F32R = mybir.dt.float32r
BF16 = mybir.dt.bfloat16
U8 = mybir.dt.uint8
U32 = mybir.dt.uint32

P = 128
HEADS = 16
HD = 16
STRIDE = 4
EPS = 1e-5
NEG = -1e30
DM = HEADS * HD
KC = DM // P
SCALE = HD ** -0.5
CH = 3
MAIN = CH * P
TAIL = 32
KEYS = MAIN + TAIL
QUAD = {0: 0, 2: 1, 3: 2, 1: 3}
MAINPOS = [0, TAIL, 0, TAIL]
TAILPOS = [MAIN, 0, MAIN, 0]
VW = HD + 1
KVPAD = P - TAIL
KVW = KEYS + 2 * KVPAD

PLACES = {
    0: "Ct", 2: "NM", 3: "OE", 5: "C00", 6: "O", 7: "C01", 9: "KV0", 11: "C10", 13: "C11", 15: "KV1",
    17: "C20", 18: "NM", 19: "OE", 21: "C21", 22: "O", 23: "KV2", 24: "LNa", 25: "C30", 27: "C31", 28: "LNb", 29: "KV3",
    30: "X0", 31: "X1", 32: "Q0", 33: "Q1", 34: "NM", 35: "OE", 36: "KT", 37: "O", 38: "V0", 39: "F0", 40: "F1",
    41: "V1", 42: "W0", 43: "W1", 44: "V2", 45: "LN2a", 47: "V3", 49: "NM", 50: "LN2b", 51: "OE", 52: "N0", 53: "N1",
    54: "O", 55: "R", 56: "RTa", 57: "RTs", 58: "RT1", 59: "RT2", 60: "RTw", 61: "Vt", 63: "RTm",
}
ROUTE_FROM = {"R": 0, "RTs": 2, "RT1": 5, "RT2": 11, "RTw": 16, "RTm": 20}
IN_PSUM = [t for t in sorted(PLACES) if PLACES[t] not in ("OE", "KT", "LNa", "LNb", "LN2a", "LN2b", "RTa", "RTs", "RT1", "RT2", "RTw")]
BANK = {t: n % 2 for n, t in enumerate(IN_PSUM)}


def count(value):
    return max(value, 0) if isinstance(value, int) else value


def present(name, q, cur, prev, load):
    if name == "NM":
        return cur if q > 0 else prev
    if name == "KT":
        return cur
    if name in ("OE", "O"):
        return cur if q == 3 else prev
    if name[0] in "FWNR" or name in ("LN2a", "LN2b"):
        return prev
    return load


def build(nc, x, ctx_in, mask, Wq, bq, Wk, bk, Wv, bv, Wo, bo, gate_w, gate_up, down, sim, out):
    NB, T, _ = x.shape
    S = ctx_in.shape[1]
    TT = T // P
    assert TT == 4 and T == 512 and S > STRIDE * MAIN and S - STRIDE * MAIN <= STRIDE * TAIL
    TAILN = [(S - STRIDE * MAIN - r + STRIDE - 1) // STRIDE for r in range(STRIDE)]
    E = gate_w.shape[0]

    CAP = NB * T + P
    xg_dram = nc.dram_tensor("xg_dram", (E * CAP + P, DM), F32).ap()
    meta_dram = nc.dram_tensor("meta_dram", (E * CAP + P, 2), F32).ap()
    mrow_dram = nc.dram_tensor("mrow_dram", (NB, STRIDE, KEYS), F32).ap()
    consts_dram = nc.dram_tensor("consts_dram", (2, T), F32).ap()

    with ExitStack() as ctx:
        def sb(name, shape, dt=F32):
            return ctx.enter_context(nc.sbuf_tensor(name, shape, dt))

        def sem(name):
            return ctx.enter_context(nc.semaphore(name))

        shared = dict(
            ident=sb("ident", [P, P]),
            ones=sb("ones", [P, P]),
            rank=sb("rank", [P, E]),
            next_slot=sb("next_slot", [P, E]),
            primary=sb("primary", [P, E]),
        )
        with ExitStack() as ctx:
            attention(nc, ctx, NB, T, S, TT, TAILN, E, CAP, x, ctx_in, mask, Wq, bq, Wk, bk, Wv, bv, Wo, bo, gate_w,
                      out, xg_dram, meta_dram, mrow_dram, consts_dram, shared)
        with ExitStack() as ctx:
            experts(nc, ctx, NB * T, E, CAP, gate_up, down, sim, out, xg_dram, meta_dram, shared)


def attention(nc, ctx, NB, T, S, TT, TAILN, E, CAP, x, ctx_in, mask, Wq, bq, Wk, bk, Wv, bv, Wo, bo, gate_w,
              out, xg_dram, meta_dram, mrow_dram, consts_dram, shared):
    ident, ones, rank, next_slot, primary = (shared[n] for n in ("ident", "ones", "rank", "next_slot", "primary"))
    NC = 2 * TT

    def sb(name, shape, dt=F32):
        return ctx.enter_context(nc.sbuf_tensor(name, shape, dt))

    def sem(name):
        return ctx.enter_context(nc.semaphore(name))

    QS = [sb(f"QS{u}", [P, HEADS // 2, T], F32R) for u in range(2)]
    KS = [sb(f"KS{u}", [P, HEADS // 2, 2 * MAIN + P], F32R) for u in range(2)]
    KT = sb("KT", [P, 4, P], F32R)
    Vm_all = [sb(f"Vm{u}", [P, STRIDE * CH * 4 * VW + 32 - VW]) for u in range(2)]
    Vt_all = [sb(f"Vt{u}", [P, STRIDE * 4 * VW + 32 - VW]) for u in range(2)]
    Vm = [v[:, 0:STRIDE * CH * 4 * VW].rearrange("p (r c j d) -> p r c j d", r=STRIDE, c=CH, j=4) for v in Vm_all]
    Vt = [v[:, 0:STRIDE * 4 * VW].rearrange("p (r j d) -> p r j d", r=STRIDE, j=4) for v in Vt_all]
    probs = sb("probs", [P, 2, 4, T])
    cin = sb("cin", [P, CH, STRIDE, DM])
    ctail = sb("ctail", [P, DM])
    xin = sb("xin", [P, TT, DM])
    xT = sb("xT", [P, KC, T])
    cT = sb("cT", [P, KC, STRIDE, KEYS])
    kvT = sb("kvT", [P, STRIDE, KVW])
    khi = sb("khi", [64, STRIDE, KEYS], F32R)
    klo = sb("klo", [64, STRIDE, KEYS], F32R)
    qhi = sb("qhi", [P, 2, T], F32R)
    qlo = sb("qlo", [P, 2, T], F32R)
    mask_u8 = sb("mask_u8", [P, CH, STRIDE], U8)
    maskt_u8 = sb("maskt_u8", [P, NB], U8)
    keep = sb("keep", [P, CH, STRIDE])
    keept = sb("keept", [P, NB])
    negmax = sb("negmax", [P, 2, TT, 4])
    negmaxT = sb("negmaxT", [4, T], F32R)
    oraw = sb("oraw", [P, T])
    rden = sb("rden", [P, TT, 4, 1])
    ctxo = sb("ctxo", [P, TT, DM])
    oT = xT
    x1 = sb("x1", [P, TT, DM])
    xn2 = sb("xn2", [P, TT, DM])
    stats = sb("stats", [P, 2, TT, 6])
    meanvar = sb("meanvar", [P, 2, TT, 2])
    vareps = sb("vareps", [P, 2, TT])
    rstd = sb("rstd", [P, 2, TT])
    before = sb("before", [P, P], BF16)
    ones_b = sb("ones_b", [P, P], BF16)
    scores = sb("scores", [P, TT, E])
    masked = sb("masked", [P, TT, E])
    choices = sb("choices", [P, NC + 1, E], BF16)
    chosen = choices[:, 0:NC, :].rearrange("p (k t) e -> p k t e", k=2)
    place = sb("place", [P, NC, E])
    small = sb("small", [P, 8, TT])
    sums = sb("sums", [P, E])
    slot = sb("slot", [P, NC])
    slot_u = sb("slot_u", [P, NC], U32)
    token = sb("token", [P, TT], U32)
    meta = sb("meta", [P, NC, 2])
    Wq_sb = sb("Wq_sb", [P, KC, DM])
    Wkv = sb("Wkv", [P, KC, STRIDE, P])
    Wo_sb = sb("Wo_sb", [P, KC, DM])
    gT = sb("gT", [P, KC, E])
    bq_sb = sb("bq_sb", [P, 2])
    bkv = sb("bkv", [P, STRIDE])
    bo_b = sb("bo_b", [P, DM])
    bv_col = sb("bv_col", [P, KC])
    bv_rep = ctxo[:, 0, :].rearrange("p (k m) -> p k m", k=KC)
    minus_half = sb("minus_half", [P, TT])
    eps = sb("eps", [P, TT])
    scrap = sb("scrap", [P, 1])
    consts = probs[0:1, 0, 0:2, :]
    mask_rows = cT[0:NB, 0, 0, :].bitcast(U8)
    mrow = kvT[0:NB, :, 0:KEYS]

    SB = 3
    psS = ctx.enter_context(nc.psum_tensor("psS", [P, SB, 512], F32))
    psT = ctx.enter_context(nc.psum_tensor("psT", [P, 2, 512], F32))
    psO = ctx.enter_context(nc.psum_tensor("psO", [P, 512], F32))
    psM = ctx.enter_context(nc.psum_tensor("psM", [P, 2, 512], F32))

    names = """w_loaded mask_loaded mrow_made mrow_stored zeroed bkv_zeroed ident_done gT_loaded bo_made bvrep_made setup_done
    consts_stored ksinit_stored bo_mm
    x_loaded c_loaded msk_loaded maskt_loaded keept_ready xres_loaded
    ct_tr ct_ready kv_mm kv_ready k_hi k_lo ks_loaded keep_ready v_tr v_ready
    ln1_stats ln1_mv ln1_eps ln1_rstd xn_ready xT_tr xT_ready q_mm q_hi q_lo qs_loaded
    s_done max_done nm_tr nmT_ready mx_loaded kt_ready st_done exp_done pv_done o_raw o_tr o_rec o_norm
    oT_tr oT_ready wo_mm xres_bias x1_ready ln2_stats ln2_mv ln2_eps ln2_rstd xn2_ready xn2T_tr xn2T_ready
    r_mm r_ready rt_exp rt_step rt_mm meta_ready x1_stored xg_stored meta_stored route_setup turn_taken odd_zeroed""".split()
    s = {n: sem(n) for n in names}

    def each_iteration(eng, body):
        body(-1, cur=False, prev=False, load=True)
        body(0, cur=True, prev=False, load=NB > 1)
        for b in range(1, min(3, NB)):
            body(b, cur=True, prev=True, load=b + 1 < NB)
        turns = max(0, (NB - 5) // 2)
        if turns:
            with eng.Fori(0, turns) as i:
                body(2 * i + 3, u=1, cur=True, prev=True, load=True)
                body(2 * i + 4, u=0, cur=True, prev=True, load=True)
        for b in range(2 * turns + 3, NB):
            body(b, cur=True, prev=True, load=b + 1 < NB)
        body(NB, cur=False, prev=True, load=False)

    def t_quad(b, u, q):
        return (b - 1, 1 - u, q + 2) if q < 2 else (b, u, q - 2)

    def o_quad(b, u, q):
        return (b - 1, 1 - u, q + 1) if q < 3 else (b, u, 0)

    def nm_quad(b, u, q):
        return (b - 1, 1 - u, 3) if q == 0 else (b, u, q - 1)

    def q_follows(b):
        return not isinstance(b, int) or b + 1 < NB

    def t_on(q, cur, prev):
        return prev if q < 2 else cur

    RT_MAX, RT_CHOSEN, RT_ALL = ROUTE_FROM["RTs"], ROUTE_FROM["RTm"], 28
    N_Q, N_KD = 26, 28
    N_W = KC * (2 + 2 * STRIDE + 3) + 5

    block = ctx.enter_context(nc.Block())

    @block.sync
    def _(sp):
        def rows_at(t, bb):
            a = t[bb] if isinstance(bb, int) else t[bass.ds(bb, 1)].rearrange("o s d -> (o s) d")
            return a.rearrange("(p t) d -> p t d", t=TT)

        def x_at(bb):
            return rows_at(x, bb)

        def o_at(bb):
            return rows_at(out[0:NB * T, :].rearrange("(b t) d -> b t d", b=NB), bb)

        def load_x(bb):
            sp.wait_ge(s["xT_tr"], count(2 * bb))
            sp.dma_start(xin[:], x_at(bb)).then_inc(s["x_loaded"], 16)

        def load_c(bb):
            src = ctx_in[bb] if isinstance(bb, int) else ctx_in[bass.ds(bb, 1)].rearrange("o s d -> (o s) d")
            m = mask[bb:bb + 1] if isinstance(bb, int) else mask[bass.ds(bb, 1)]
            tails = [(32 * QUAD[r], TAILN[r], STRIDE * MAIN + r) for r in range(STRIDE)]
            sp.wait_ge(s["ct_tr"], count(9 * bb))
            sp.dma_start(cin[:], src[0:STRIDE * MAIN, :].rearrange("(c p r) d -> p c r d", p=P, r=STRIDE)
                         ).then_inc(s["c_loaded"], 16)
            for p0, nr, first in tails:
                keys = slice(first, first + STRIDE * (nr - 1) + 1, STRIDE)
                sp.dma_start(ctail[p0:p0 + nr, :], src[keys, :]).then_inc(s["c_loaded"], 16)
            sp.dma_start(mask_u8[:], m[:, 0:STRIDE * MAIN].rearrange("o (c p r) -> (o p) c r", p=P, r=STRIDE)
                         ).then_inc(s["msk_loaded"], 16)

        sp.dma_start(mask_rows[:, 0:S], mask).then_inc(s["mask_loaded"], 16)
        sp.wait_ge(s["setup_done"], 4)
        load_c(0)
        load_x(0)
        for r in range(STRIDE):
            first = STRIDE * MAIN + r
            keys = mask[:, first:first + STRIDE * (TAILN[r] - 1) + 1:STRIDE]
            sp.dma_start(maskt_u8[32 * QUAD[r]:32 * QUAD[r] + TAILN[r], :], keys.rearrange("b p -> p b"),
                         allow_slow_non_contiguous=True).then_inc(s["maskt_loaded"], 16)
        n = 0
        for k in range(KC):
            rows = slice(k * P, (k + 1) * P)
            sp.dma_start(Wq_sb[:, k, :], Wq[rows, :]).then_inc(s["w_loaded"], 16)
            sp.dma_start(Wo_sb[:, k, :], Wo[rows, :]).then_inc(s["w_loaded"], 16)
            n += 2
            for r in range(STRIDE):
                for half, W in ((0, Wk), (64, Wv)):
                    src = W[rows, :].rearrange("p (j r d) -> p j r d", r=STRIDE, d=HD)[:, :, r, :]
                    dst = Wkv[:, k, r, half:half + 64].rearrange("p (j d) -> p j d", d=HD)
                    sp.dma_start(dst, src).then_inc(s["w_loaded"], 16)
                    n += 1
            sp.dma_start(xn2[0:E, k, 0:P], gate_w[:, rows]).then_inc(s["w_loaded"], 16)
            sp.dma_start(bq_sb[:, k:k + 1], bq[rows].rearrange("(p a) -> p a", a=1)).then_inc(s["w_loaded"], 16)
            sp.dma_start(bv_col[:, k:k + 1], bv[rows].rearrange("(p a) -> p a", a=1)).then_inc(s["w_loaded"], 16)
            n += 3
        sp.wait_ge(s["bkv_zeroed"], 1)
        for j in range(4):
            sp.dma_start(bkv[16 * j:16 * j + 16, :],
                         bk[64 * j:64 * j + 64].rearrange("(r d) -> d r", d=HD), allow_slow_non_contiguous=True).then_inc(s["w_loaded"], 16)
        sp.dma_start(x1[:, 0, :], bo.rearrange("(a n) -> a n", a=1).broadcast_to([P, DM])).then_inc(s["w_loaded"], 16)
        n += 5
        assert n == N_W, n
        sp.wait_ge(s["mrow_made"], 1 + 2 * STRIDE)
        sp.dma_start(mrow_dram, mrow).then_inc(s["mrow_stored"], 16)
        sp.wait_ge(s["zeroed"], 2)
        sp.dma_start(consts_dram.rearrange("(o a) n -> o a n", o=1), consts).then_inc(s["consts_stored"], 16)
        sp.wait_ge(s["consts_stored"], 16)
        sp.wait_ge(s["zeroed"], 4)
        sp.wait_ge(s["odd_zeroed"], 2)
        for u in range(2):
            for a in range(2):
                sp.dma_start(KS[u][64 * a + 48:64 * a + 49, :, a * 480:a * 480 + KEYS].bitcast(F32),
                             consts_dram[1:2, 0:KEYS].unsqueeze(1).broadcast_to([1, HEADS // 2, KEYS])
                             ).then_inc(s["ksinit_stored"], 16)
        sp.wait_ge(s["mrow_stored"], 16)

        def body(b, cur, prev, load, u=None):
            u = b % 2 if u is None else u
            v = 1 - u
            ahead = load and not (isinstance(b, int) and b + 2 >= NB)

            def max_rows(q):
                if present("NM", q, cur, prev, load):
                    bn, un, qn = nm_quad(b, u, q)
                    sp.wait_ge(s["nmT_ready"], count(4 * bn + qn + 1))
                    for a in range(2):
                        sp.dma_start(QS[un][64 * a + 48:64 * a + 49, 2 * qn:2 * qn + 1, :].bitcast(F32),
                                     negmaxT[a:a + 1, :].bitcast(F32)).then_inc(s["mx_loaded"], 16)
                        sp.dma_start(QS[un][64 * a + 48:64 * a + 49, 2 * qn + 1:2 * qn + 2, :].bitcast(F32),
                                     negmaxT[2 + a:3 + a, :].bitcast(F32)).then_inc(s["mx_loaded"], 16)

            if prev:
                sp.wait_ge(s["x1_stored"], count(16 * (b - 1)))
                sp.dma_start(x1[:], x_at(b - 1)).then_inc(s["xres_loaded"], 16)
            max_rows(0)
            max_rows(1)
            if load:
                sp.wait_ge(s["st_done"], count(52 * b))
                for a in range(2):
                    msrc = mrow_dram[b + 1:b + 2] if isinstance(b, int) else mrow_dram[bass.ds(b + 1, 1)]
                    for i in range(2):
                        sp.dma_start(KS[v][64 * a + 49:64 * a + 50, i::2, a * 480:a * 480 + KEYS].bitcast(F32),
                                     msrc[:, a + 2 * i:a + 2 * i + 1, :].broadcast_to([1, 4, KEYS])
                                     ).then_inc(s["ks_loaded"], 16)
                if ahead and cur:
                    load_c(b + 2)
                sp.wait_ge(s["k_lo"], count(4 * (b + 2)))
                for a in range(2):
                    if a == 1:
                        max_rows(2)
                    for j in range(4):
                        for x_, part in enumerate((khi, klo, khi)):
                            sp.dma_start(KS[v][64 * a + 16 * x_:64 * a + 16 * x_ + 16, 2 * j:2 * j + 2,
                                               a * 480:a * 480 + KEYS].bitcast(F32),
                                         part[16 * j:16 * j + 16, a::2, :].bitcast(F32)).then_inc(s["ks_loaded"], 16)
            if not load:
                max_rows(2)
            if ahead and cur:
                load_x(b + 2)
            if load:
                sp.wait_ge(s["q_lo"], count(2 * (b + 2)))
                sp.wait_ge(s["st_done"], count(52 * b))
                for g in range(8):
                    if g == 4:
                        max_rows(3)
                    for x_, part in enumerate((qhi, qhi, qlo)):
                        p0 = 64 * (g % 2) + 16 * x_
                        sp.dma_start(QS[v][p0:p0 + 16, g // 2::4, :].bitcast(F32),
                                     part[16 * g:16 * g + 16, :, :].bitcast(F32)).then_inc(s["qs_loaded"], 16)
                for a in range(2):
                    sp.dma_start(QS[v][64 * a + 48:64 * a + 49, :, :].bitcast(F32),
                                 consts_dram[0:1, :].unsqueeze(1).broadcast_to([1, HEADS // 2, T])
                                 ).then_inc(s["qs_loaded"], 16)
            if ahead and not cur:
                load_c(b + 2)
                load_x(b + 2)
            if not load:
                max_rows(3)
            if prev:
                sp.wait_ge(s["xn2_ready"], count(4 * b))
                sp.dma_start(o_at(b - 1), x1[:]).then_inc(s["x1_stored"], 16)

        each_iteration(sp, body)
        sp.wait_ge(s["x1_stored"], 16 * NB)
        sp.wait_ge(s["xg_stored"], 16 * NC * NB)
        sp.wait_ge(s["meta_stored"], 16 * NC * NB)

    @block.gpsimd
    def _(pool):
        pool.memset(bkv[:], 0.0).then_inc(s["bkv_zeroed"], 1)
        pool.memset(ident[:], 0.0).then_inc(s["ident_done"], 1)
        pool.wait_ge(s["ident_done"], 1)
        pool.affine_select(out=ident[:], in_=ident[:], compare_op=ALU.not_equal, fill=1.0, base=0,
                           pattern=[[-1, P]], channel_multiplier=1).then_inc(s["ident_done"], 1)
        pool.iota(rank[:], [[-1, E]], base=E, channel_multiplier=0, allow_small_or_imprecise_dtypes=True
                  ).then_inc(s["route_setup"], 1)
        pool.iota(next_slot[:], [[CAP, E]], base=0, channel_multiplier=0, allow_small_or_imprecise_dtypes=True
                  ).then_inc(s["route_setup"], 1)
        pool.iota(token[:], [[1, TT]], base=0, channel_multiplier=TT).then_inc(s["route_setup"], 1)
        pool.memset(primary[:], 0.0).then_inc(s["route_setup"], 1)
        pool.memset(ones[:], 1.0).then_inc(s["route_setup"], 1)
        pool.memset(ones_b[:], 1.0).then_inc(s["route_setup"], 1)
        pool.memset(choices[:, NC, :], 0.0).then_inc(s["route_setup"], 1)
        pool.wait_ge(s["route_setup"], 7)
        pool.affine_select(out=before[:], in_=ones_b[:], compare_op=ALU.is_gt, fill=0.0, base=0,
                           pattern=[[1, P]], channel_multiplier=-1).then_inc(s["route_setup"], 1)
        pool.memset(minus_half[:], -0.5).then_inc(s["setup_done"], 1)
        pool.memset(eps[:], EPS).then_inc(s["setup_done"], 1)
        pool.memset(ctail[:], 0.0).then_inc(s["setup_done"], 1)
        pool.memset(maskt_u8[:], 1).then_inc(s["setup_done"], 1)
        pool.wait_ge(s["setup_done"], 4)
        pool.memset(QS[1][:].bitcast(F32), 1.0).then_inc(s["odd_zeroed"], 1)
        pool.memset(KS[1][:].bitcast(F32), 0.0).then_inc(s["odd_zeroed"], 1)

        def body(b, cur, prev, load, u=None):
            if load:
                pool.wait_ge(s["ln1_mv"], count(4 * (b + 2)))
                pool.wait_ge(s["xn_ready"], count(4 * (b + 1)))
                pool.tensor_tensor(vareps[:, 0, :], meanvar[:, 0, :, 1], eps[:], ALU.add).then_inc(s["ln1_eps"], 1)
                pool.wait_ge(s["ln1_eps"], count(b + 2))
                pool.tensor_tensor(rstd[:, 0, :], vareps[:, 0, :], minus_half[:], ALU.pow).then_inc(s["ln1_rstd"], 1)
            if prev:
                pool.wait_ge(s["xres_loaded"], count(16 * b))
                pool.wait_ge(s["bo_made"], 1)
                for t in range(TT):
                    pool.tensor_tensor(x1[:, t, :], x1[:, t, :], bo_b[:], ALU.add).then_inc(s["xres_bias"], 1)
                pool.wait_ge(s["ln2_mv"], count(4 * b))
                pool.wait_ge(s["xn2_ready"], count(4 * (b - 1)))
                pool.tensor_tensor(vareps[:, 1, :], meanvar[:, 1, :, 1], eps[:], ALU.add).then_inc(s["ln2_eps"], 1)
                pool.wait_ge(s["ln2_eps"], count(b))
                pool.tensor_tensor(rstd[:, 1, :], vareps[:, 1, :], minus_half[:], ALU.pow).then_inc(s["ln2_rstd"], 1)
                pool.wait_ge(s["xn2_ready"], count(4 * b))
                pool.wait_ge(s["meta_ready"], count(b))
                pool.wait_ge(s["turn_taken"], count(b - 1))
                pool.tensor_tensor(scrap[:], eps[:, 0:1], eps[:, 0:1], ALU.add).then_inc(s["turn_taken"], 1)
                for i in range(NC):
                    at = bass.IndirectOffsetOnAxis(ap=slot_u[:, i:i + 1], axis=0)
                    pool.indirect_dma_start(xg_dram, at, xn2[:, i % TT, :], None).then_inc(s["xg_stored"], 16)
                    at = bass.IndirectOffsetOnAxis(ap=slot_u[:, i:i + 1], axis=0)
                    pool.indirect_dma_start(meta_dram, at, meta[:, i, :], None).then_inc(s["meta_stored"], 16)

        each_iteration(pool, body)
        pool.wait_ge(s["turn_taken"], NB)

    @block.scalar
    def _(act):
        def body(b, cur, prev, load, u=None):
            u = b % 2 if u is None else u
            for t in range(64):
                q, c, k = t // 16, t // 4 % 4, t % 4
                if t_on(q, cur, prev) and (c < CH or k == 0):
                    bt, ut, qt = t_quad(b, u, q)
                    n = 13 * qt + 4 * c + k
                    step = 16 * bt + 4 * qt + c
                    act.wait_ge(s["st_done"], count(52 * bt + n + 1))
                    if k == 0:
                        if not (isinstance(step, int) and step < 2):
                            act.wait_ge(s["pv_done"], count(step - 1))
                    act.activation(probs[:, c % 2, k, :], psT[:, n % 2, :], ACT.Exp, scale=SCALE
                                   ).then_inc(s["exp_done"], 1)
                name = PLACES.get(t)
                if name and present(name, q, cur, prev, load):
                    task(name, t, q, b, u)

        def task(name, t, q, b, u):
            ps = psM[:, BANK[t], :] if t in BANK else None
            n = b + 1
            if name == "Ct":
                if isinstance(b, int) and b < 0:
                    act.wait_ge(s["mrow_made"], 1 + 2 * STRIDE)
                act.wait_ge(s["ct_tr"], count(9 * n + 1))
                act.wait_ge(s["kv_mm"], count(4 * n))
                pv = ps[:, 0:256].rearrange("p (k g c) -> p k g c", k=KC, g=4)
                act.activation(cT[:, :, 0::2, MAIN:KEYS], pv[:, :, 0:2, :], ACT.Copy)
                act.activation(cT[:, :, 3, 0:TAIL], pv[:, :, 2, :], ACT.Copy)
                act.activation(cT[:, :, 1, 0:TAIL], pv[:, :, 3, :], ACT.Copy).then_inc(s["ct_ready"], 1)
            elif name[0] == "C":
                r, kk = int(name[1]), int(name[2])
                act.wait_ge(s["ct_tr"], count(9 * n + 2 + 2 * r + kk))
                act.activation(cT[:, kk, r, MAINPOS[r]:MAINPOS[r] + MAIN], ps[:, 0:MAIN], ACT.Copy
                               ).then_inc(s["ct_ready"], 1)
            elif name[:2] == "KV":
                r = int(name[2])
                act.wait_ge(s["kv_mm"], count(4 * n + r + 1))
                act.wait_ge(s["k_lo"], count(4 * n))
                act.wait_ge(s["v_tr"], count(5 * n))
                if isinstance(b, int) and b < 0:
                    act.wait_ge(s["zeroed"], 3)
                    act.wait_ge(s["w_loaded"], 16 * N_W)
                    act.wait_ge(s["mrow_stored"], 16)
                act.activation(kvT[:, r, KVPAD:KVPAD + KEYS], ps[:, 0:KEYS], ACT.Identity, bias=bkv[:, r:r + 1]
                               ).then_inc(s["kv_ready"], 1)
            elif name == "NM":
                bn, un, qn = nm_quad(b, u, q)
                act.wait_ge(s["nm_tr"], count(4 * bn + qn + 1))
                act.wait_ge(s["mx_loaded"], count(64 * (4 * bn + qn)))
                act.activation(negmaxT[:], ps[0:4, :], ACT.Copy).then_inc(s["nmT_ready"], 1)
            elif name == "OE":
                bo_, uo, qo = o_quad(b, u, q)
                act.wait_ge(s["pv_done"], count(16 * bo_ + 4 * qo + 4))
                act.wait_ge(s["o_tr"], count(4 * bo_ + qo))
                act.activation(oraw[:], psO[:], ACT.Copy).then_inc(s["o_raw"], 1)
            elif name[0] == "X":
                kk = int(name[1])
                act.wait_ge(s["xT_tr"], count(2 * n + kk + 1))
                act.wait_ge(s["q_mm"], count(2 * n))
                act.wait_ge(s["r_mm"], count(b - 1))
                act.activation(xT[:, kk, :], ps, ACT.Copy).then_inc(s["xT_ready"], 1)
            elif name[0] == "Q":
                m = int(name[1])
                act.wait_ge(s["q_mm"], count(2 * n + m + 1))
                act.wait_ge(s["qs_loaded"], count(16 * N_Q * n))
                act.activation(qhi[:, m, :], ps, ACT.Identity, bias=bq_sb[:, m:m + 1]).then_inc(s["q_hi"], 1)
            elif name[0] == "F":
                kk = int(name[1])
                act.wait_ge(s["oT_tr"], count(2 * (b - 1) + kk + 1))
                act.wait_ge(s["q_mm"], count(2 * (b + 2) if q_follows(b) else 2 * NB))
                act.activation(oT[:, kk, :], ps, ACT.Copy).then_inc(s["oT_ready"], 1)
            elif name[0] == "N":
                kk = int(name[1])
                act.wait_ge(s["xn2T_tr"], count(2 * (b - 1) + kk + 1))
                act.wait_ge(s["wo_mm"], count(2 * b))
                act.activation(oT[:, kk, :], ps, ACT.Copy).then_inc(s["xn2T_ready"], 1)
            elif name == "RTa":
                act.wait_ge(s["rt_step"], count(RT_ALL * (b - 1) + RT_MAX))
                act.activation(scores[:], scores[:], ACT.Exp).then_inc(s["rt_exp"], 1)

        each_iteration(act, body)

    @block.tensor
    def _(pe):
        last_user = {}

        pe.wait_ge(s["w_loaded"], 16 * N_W)
        pe.wait_ge(s["ident_done"], 2)
        for k in range(KC):
            mm = pe.transpose(psO[:, k * 8:k * 8 + E], xn2[0:E, k, 0:P], ident[0:E, 0:E])
        mm.then_inc(s["bo_mm"], 1)
        pe.wait_ge(s["bvrep_made"], 1)
        for k in range(KC):
            mm = pe.matmul(psM[:, 0, 0:DM], bv_rep[:, k, :], Wo_sb[:, k, :], start=(k == 0), stop=(k == KC - 1))
        mm.then_inc(s["bo_mm"], 1)
        pe.wait_ge(s["bo_made"], 1)

        def body(b, cur, prev, load, u=None):
            u = b % 2 if u is None else u
            for t in range(64):
                q, c, k = t // 16, t // 4 % 4, t % 4
                if cur:
                    if t == 0:
                        pe.wait_ge(s["ksinit_stored"], 64)
                        pe.wait_ge(s["ks_loaded"], count(16 * N_KD * (b + 1)))
                        pe.wait_ge(s["qs_loaded"], count(16 * N_Q * (b + 1)))
                    w, a = 2 * q + k // 2, k % 2
                    n = 64 * b + t
                    back = SB if t >= SB else min(d for d in range(1, 64) if (t - d) % 64 % SB == t)
                    if not (isinstance(n, int) and n < back):
                        pe.wait_ge(s["max_done"], count(n - back + 1))
                    pe.matmul(psS[:, t % SB, 0:KEYS], QS[u][:, w, c * P:(c + 1) * P],
                              KS[u][:, w, a * 480:a * 480 + KEYS], start=True, stop=True).then_inc(s["s_done"], 1)
                if t_on(q, cur, prev) and (c < CH or k == 0):
                    bt, ut, qt = t_quad(b, u, q)
                    n = 13 * qt + 4 * c + k
                    if c == 0 and k == 0:
                        pe.wait_ge(s["mx_loaded"], count(64 * (4 * bt + qt + 1)))
                    if not (isinstance(bt, int) and 52 * bt + n < 2):
                        pe.wait_ge(s["exp_done"], count(52 * bt + n - 1))
                    w, a = 2 * qt + k // 2, k % 2
                    o = psT[:, n % 2, :]
                    if c < CH:
                        pe.matmul(o, KS[ut][:, w, a * (MAIN + P) + c * P:a * (MAIN + P) + (c + 1) * P],
                                  QS[ut][:, w, :], start=True, stop=True).then_inc(s["st_done"], 1)
                    else:
                        pe.matmul(o, KS[ut][:, w, MAIN:MAIN + P], QS[ut][:, w, :], start=True, stop=False)
                        if qt == 0:
                            pe.wait_ge(s["kt_ready"], count(bt + 1))
                        pe.matmul(o, KT[:, qt, :], QS[ut][:, w + 1, :], start=False, stop=True
                                  ).then_inc(s["st_done"], 1)
                if k == 1:
                    qp = q if c else q - 1
                    bb, uu, cp = b, u, (c - 1) % 4
                    if qp < 0:
                        on = prev
                        bp, up, qv = b - 1, 1 - u, 1
                    else:
                        on = t_on(qp, cur, prev)
                        bp, up, qv = t_quad(b, u, qp)
                    if on:
                        pv(bp, up, qv, cp)
                name = PLACES.get(t)
                if name and present(name, q, cur, prev, load):
                    if t in BANK:
                        bank = BANK[t]
                        if bank in last_user:
                            nm, per, shift, off = last_user[bank]
                            pe.wait_ge(s[nm], count(per * (b + shift) + off))
                        last_user[bank] = task(name, t, q, b, u)
            for bank in last_user:
                nm, per, shift, off = last_user[bank]
                last_user[bank] = (nm, per, shift - 1, off)

        def pv(bt, ut, qt, c):
            pe.wait_ge(s["exp_done"], count(52 * bt + 13 * qt + 4 * c + (4 if c < CH else 1)))
            if c == 0:
                pe.wait_ge(s["v_ready"], count(5 * (bt + 1)))
                if not (isinstance(bt, int) and 4 * bt + qt < 1):
                    pe.wait_ge(s["o_raw"], count(4 * bt + qt))
            for r in range(STRIDE):
                at = ((r * CH + c) * 4 + qt if c < CH else r * 4 + qt) * VW
                w = (Vm_all if c < CH else Vt_all)[ut][:, at:at + 32]
                mm = pe.matmul(psO[32 * r:32 * r + 32, :], w, probs[:, c % 2, r if c < CH else 0, :],
                               start=(c == 0), stop=(c == CH))
            mm.then_inc(s["pv_done"], 1)

        def task(name, t, q, b, u):
            ps = psM[:, BANK[t], :]
            n = b + 1
            if name == "Ct":
                pe.wait_ge(s["c_loaded"], count(16 * 5 * (n + 1)))
                for kk in range(KC):
                    mm = pe.transpose(ps[:, kk * P:(kk + 1) * P], ctail[:, kk * P:(kk + 1) * P], ident[:])
                mm.then_inc(s["ct_tr"], 1)
                return "ct_ready", 9, 1, 1
            if name[0] == "C":
                r, kk = int(name[1]), int(name[2])
                for ch in range(CH):
                    mm = pe.transpose(ps[:, ch * P:(ch + 1) * P], cin[:, ch, r, kk * P:(kk + 1) * P], ident[:])
                mm.then_inc(s["ct_tr"], 1)
                return "ct_ready", 9, 1, 2 + 2 * r + kk
            if name[:2] == "KV":
                r = int(name[2])
                pe.wait_ge(s["ct_ready"], count(9 * n + 3 + 2 * r))
                for kk in range(KC):
                    mm = pe.matmul(ps[:, 0:KEYS], Wkv[:, kk, r, :], cT[:, kk, r, :], start=(kk == 0), stop=(kk == KC - 1))
                mm.then_inc(s["kv_mm"], 1)
                return "kv_ready", 4, 1, r + 1
            if name == "NM":
                bn, un, qn = nm_quad(b, u, q)
                pe.wait_ge(s["max_done"], count(64 * bn + 16 * qn + 16))
                for tt in range(TT):
                    mm = pe.transpose(ps[0:4, tt * P:(tt + 1) * P], negmax[:, qn % 2, tt, :], ident[:])
                mm.then_inc(s["nm_tr"], 1)
                return "nmT_ready", 4, (-1 if q == 0 else 0), qn + 1
            if name == "O":
                bo_, uo, qo = o_quad(b, u, q)
                pe.wait_ge(s["o_raw"], count(4 * bo_ + qo + 1))
                for tt in range(TT):
                    mm = pe.transpose(ps[:, tt * P:(tt + 1) * P], oraw[:, tt * P:(tt + 1) * P], ident[:])
                mm.then_inc(s["o_tr"], 1)
                return "o_norm", 4, (-1 if q < 3 else 0), qo + 1
            if name[0] == "X":
                kk = int(name[1])
                pe.wait_ge(s["xn_ready"], count(4 * (n + 1)))
                for tt in range(TT):
                    mm = pe.transpose(ps[:, tt * P:(tt + 1) * P], xin[:, tt, kk * P:(kk + 1) * P], ident[:])
                mm.then_inc(s["xT_tr"], 1)
                return "xT_ready", 2, 1, kk + 1
            if name[0] == "Q":
                m = int(name[1])
                pe.wait_ge(s["xT_ready"], count(2 * (n + 1)))
                for kk in range(KC):
                    mm = pe.matmul(ps, Wq_sb[:, kk, m * P:(m + 1) * P], xT[:, kk, :], start=(kk == 0), stop=(kk == KC - 1))
                mm.then_inc(s["q_mm"], 1)
                return "q_lo", 2, 1, m + 1
            if name == "Vt":
                pe.wait_ge(s["kv_ready"], count(4 * (n + 1)))
                for r in range(STRIDE):
                    at = KVPAD + TAILPOS[r] - 32 * QUAD[r]
                    mm = pe.transpose(ps[:, r * P:(r + 1) * P], kvT[:, r, at:at + P], ident[:])
                mm.then_inc(s["v_tr"], 1)
                return "v_ready", 5, 1, 5
            if name[0] == "V":
                r = int(name[1])
                pe.wait_ge(s["kv_ready"], count(4 * n + r + 1))
                for ch in range(CH):
                    at = KVPAD + MAINPOS[r] + ch * P
                    mm = pe.transpose(ps[:, ch * P:(ch + 1) * P], kvT[:, r, at:at + P], ident[:])
                mm.then_inc(s["v_tr"], 1)
                return "v_ready", 5, 1, r + 1
            if name[0] == "F":
                kk = int(name[1])
                pe.wait_ge(s["o_norm"], count(4 * b))
                for tt in range(TT):
                    mm = pe.transpose(ps[:, tt * P:(tt + 1) * P], ctxo[:, tt, kk * P:(kk + 1) * P], ident[:])
                mm.then_inc(s["oT_tr"], 1)
                return "oT_ready", 2, -1, kk + 1
            if name[0] == "W":
                h = int(name[1])
                pe.wait_ge(s["oT_ready"], count(2 * b))
                for i in range(2):
                    tt = 2 * h + i
                    for kk in range(KC):
                        mm = pe.matmul(ps[:, i * DM:(i + 1) * DM], oT[:, kk, tt * P:(tt + 1) * P], Wo_sb[:, kk, :],
                                       start=(kk == 0), stop=(kk == KC - 1))
                mm.then_inc(s["wo_mm"], 1)
                return "x1_ready", 2, -1, h + 1
            if name[0] == "N":
                kk = int(name[1])
                pe.wait_ge(s["xn2_ready"], count(4 * b))
                for tt in range(TT):
                    mm = pe.transpose(ps[:, tt * P:(tt + 1) * P], xn2[:, tt, kk * P:(kk + 1) * P], ident[:])
                mm.then_inc(s["xn2T_tr"], 1)
                return "xn2T_ready", 2, -1, kk + 1
            if name == "RTm":
                pe.wait_ge(s["rt_step"], count(RT_ALL * (b - 1) + RT_CHOSEN))
                pe.wait_ge(s["route_setup"], 8)
                oh = choices[:].rearrange("p c e -> p (c e)")
                for i in range(NC + 1):
                    mm = pe.matmul(ps[:, i * E:(NC + 1) * E], before[:] if i == 0 else ones_b[:],
                                   oh[:, 0:(NC + 1 - i) * E], start=(i == 0), stop=(i == NC))
                mm.then_inc(s["rt_mm"], 1)
                return "meta_ready", 1, -1, 1
            assert name == "R"
            pe.wait_ge(s["xn2T_ready"], count(2 * b))
            for tt in range(TT):
                for kk in range(KC):
                    mm = pe.matmul(ps[:, tt * E:(tt + 1) * E], oT[:, kk, tt * P:(tt + 1) * P], gT[:, kk, :],
                                   start=(kk == 0), stop=(kk == KC - 1))
            mm.then_inc(s["r_mm"], 1)
            return "r_ready", 1, -1, 1

        each_iteration(pe, body)

    @block.vector
    def _(dve):
        dve.memset(consts[:, 0, :], 0.0).then_inc(s["zeroed"], 1)
        dve.memset(consts[:, 1, :], 1.0).then_inc(s["zeroed"], 1)
        dve.memset(kvT[:], NEG).then_inc(s["mrow_made"], 1)
        dve.wait_ge(s["mrow_made"], 1)
        dve.wait_ge(s["mask_loaded"], 16)
        for r in range(STRIDE):
            dve.tensor_scalar(mrow[:, r, MAINPOS[r]:MAINPOS[r] + MAIN], mask_rows[:, r:STRIDE * MAIN:STRIDE], NEG, None,
                              ALU.mult).then_inc(s["mrow_made"], 1)
            nr = TAILN[r]
            first = STRIDE * MAIN + r
            dve.tensor_scalar(mrow[:, r, TAILPOS[r]:TAILPOS[r] + nr],
                              mask_rows[:, first:first + STRIDE * (nr - 1) + 1:STRIDE], NEG, None,
                              ALU.mult).then_inc(s["mrow_made"], 1)
        dve.wait_ge(s["mrow_stored"], 16)
        dve.memset(kvT[:], 0.0).then_inc(s["zeroed"], 1)
        dve.wait_ge(s["w_loaded"], 16 * N_W)
        dve.tensor_copy(bv_rep[:], bv_col[:].unsqueeze(2).broadcast_to([P, KC, P])).then_inc(s["bvrep_made"], 1)
        dve.wait_ge(s["bo_mm"], 1)
        dve.tensor_copy(gT[:], psO[:, 0:KC * 8].rearrange("p (k e) -> p k e", e=8)[:, :, 0:E])
        dve.wait_ge(s["bo_mm"], 2)
        dve.tensor_tensor(bo_b[:], psM[:, 0, 0:DM], x1[:, 0, :], ALU.add).then_inc(s["bo_made"], 1)
        dve.wait_ge(s["maskt_loaded"], 16 * STRIDE)
        dve.tensor_scalar(keept[:], maskt_u8[:], -1.0, 1.0, ALU.mult, ALU.add).then_inc(s["keept_ready"], 1)
        dve.memset(QS[0][:].bitcast(F32), 1.0)
        dve.memset(KS[0][:].bitcast(F32), 0.0).then_inc(s["zeroed"], 1)
        dve.memset(KT[:].bitcast(F32), 0.0)
        for v in Vm_all + Vt_all:
            dve.memset(v[:], 0.0)

        def body(b, cur, prev, load, u=None):
            u = b % 2 if u is None else u
            for t in range(64):
                q, c, k = t // 16, t // 4 % 4, t % 4
                norm = PLACES.get(t - 1) if PLACES.get(t - 1) in ("LNa", "LN2a") else None
                norm = norm if norm and present(norm, q, cur, prev, load) else None
                if norm == "LNa":
                    dve.wait_ge(s["ln1_stats"], count(4 * (b + 2)))
                elif norm:
                    dve.wait_ge(s["ln2_stats"], count(4 * b))
                if cur:
                    dve.wait_ge(s["s_done"], count(64 * b + t + 1))
                    if t % 16 == 0:
                        if not (isinstance(b, int) and 4 * b + q < 2):
                            dve.wait_ge(s["nm_tr"], count(4 * b + q - 1))
                    dve.tensor_reduce(negmax[:, q % 2, c, k:k + 1], psS[:, t % SB, 0:KEYS], AX, ALU.max, negate=True
                                      ).then_inc(s["max_done"], 1)
                if norm:
                    layer_norm_mean(*((0, "ln1") if norm == "LNa" else (1, "ln2")))
                name = PLACES.get(t)
                if name and present(name, q, cur, prev, load):
                    task(name, t, q, b, u)

        def layer_norm_stats(src, i, pre):
            for tt in range(TT):
                dve.bn_stats(stats[:, i, tt, :], src[:, tt, :]).then_inc(s[pre + "_stats"], 1)

        def layer_norm_mean(i, pre):
            for tt in range(TT):
                dve.bn_aggr(meanvar[:, i, tt, :], stats[:, i, tt, :]).then_inc(s[pre + "_mv"], 1)

        def layer_norm_apply(dst, src, i, done):
            for tt in range(TT):
                dve.tensor_scalar(dst[:, tt, :], src[:, tt, :], meanvar[:, i, tt, 0:1], rstd[:, i, tt:tt + 1],
                                  ALU.subtract, ALU.mult).then_inc(s[done], 1)

        def task(name, t, q, b, u):
            ps = psM[:, BANK[t], :] if t in BANK else None
            n = b + 1
            v = 1 - u
            if name == "LNa":
                dve.wait_ge(s["x_loaded"], count(16 * (n + 1)))
                layer_norm_stats(xin, 0, "ln1")
            elif name == "LNb":
                dve.wait_ge(s["ln1_rstd"], count(n + 1))
                layer_norm_apply(xin, xin, 0, "xn_ready")
            elif name == "LN2a":
                dve.wait_ge(s["x1_ready"], count(2 * b))
                layer_norm_stats(x1, 1, "ln2")
            elif name == "LN2b":
                dve.wait_ge(s["ln2_rstd"], count(b))
                dve.wait_ge(s["xg_stored"], count(16 * NC * (b - 1)))
                dve.wait_ge(s["xn2T_tr"], count(2 * (b - 1)))
                layer_norm_apply(xn2, x1, 1, "xn2_ready")
            elif name == "KT":
                dve.wait_ge(s["st_done"], count(52 * b))
                src = KS[u][:, 1::2, MAIN:MAIN + P].rearrange("p j (g c) -> p j g c", g=4)[:, :, 0::3, :]
                dve.tensor_copy(KT[:].rearrange("p j (g c) -> p j g c", g=4)[:, :, 1:3, :], src.bitcast(F32)
                                ).then_inc(s["kt_ready"], 1)
            elif name[:2] == "KV":
                r = int(name[2])
                if r == 0:
                    dve.wait_ge(s["msk_loaded"], count(16 * (n + 1)))
                    dve.wait_ge(s["v_ready"], count(5 * n))
                    dve.tensor_scalar(keep[:], mask_u8[:], -1.0, 1.0, ALU.mult, ALU.add).then_inc(s["keep_ready"], 1)
                    dve.wait_ge(s["ks_loaded"], count(16 * N_KD * n))
                dve.wait_ge(s["kv_ready"], count(4 * n + r + 1))
                src = kvT[0:64, r, KVPAD:KVPAD + KEYS]
                dve.tensor_copy(khi[:, r, :], src).then_inc(s["k_hi"], 1)
                dve.wait_ge(s["k_hi"], count(4 * n + r + 1))
                dve.tensor_tensor(klo[:, r, :], src, khi[:, r, :].bitcast(F32), ALU.subtract).then_inc(s["k_lo"], 1)
            elif name[0] == "Q":
                m = int(name[1])
                dve.wait_ge(s["q_hi"], count(2 * n + m + 1))
                dve.scalar_tensor_tensor(out=qlo[:, m, :], in0=ps, scalar=bq_sb[:, m:m + 1],
                                         in1=qhi[:, m, :].bitcast(F32), op0=ALU.add, op1=ALU.subtract
                                         ).then_inc(s["q_lo"], 1)
            elif name == "Vt":
                dve.wait_ge(s["keept_ready"], 1)
                dve.wait_ge(s["v_tr"], count(5 * n + 5))
                kept = keept[:, n:n + 1] if isinstance(n, int) else keept[:, bass.ds(n, 1)]
                for r in range(STRIDE):
                    rows = slice(32 * QUAD[r], 32 * QUAD[r] + 32)
                    src = ps[rows, r * P + 64:(r + 1) * P].rearrange("p (j d) -> p j d", d=HD)
                    last = dve.tensor_scalar(Vt[v][rows, r, :, 0:HD], src, kept[rows, :], None, ALU.mult)
                    last = dve.tensor_copy(Vt[v][rows, r, :, HD:HD + 1], kept[rows, :].unsqueeze(2).broadcast_to([32, 4, 1]))
                last.then_inc(s["v_ready"], 1)
            elif name[0] == "V":
                r = int(name[1])
                dve.wait_ge(s["v_tr"], count(5 * n + r + 1))
                dve.wait_ge(s["keep_ready"], count(n + 1))
                if r == 0 and not (isinstance(b, int) and b < 1):
                    dve.wait_ge(s["pv_done"], count(16 * b))
                src = ps[:, 0:MAIN].rearrange("p (c h j d) -> p c h j d", c=CH, h=2, d=HD)[:, :, 1, :, :]
                kr = keep[:, :, r].unsqueeze(2).unsqueeze(3).broadcast_to([P, CH, 4, HD])
                dve.tensor_tensor(Vm[v][:, r, :, :, 0:HD], src, kr, ALU.mult)
                dve.tensor_copy(Vm[v][:, r, :, :, HD:HD + 1],
                                keep[:, :, r].unsqueeze(2).unsqueeze(3).broadcast_to([P, CH, 4, 1])
                                ).then_inc(s["v_ready"], 1)
            elif name == "O":
                bo_, uo, qo = o_quad(b, u, q)
                dve.wait_ge(s["o_tr"], count(4 * bo_ + qo + 1))
                if qo == 0:
                    dve.wait_ge(s["oT_tr"], count(2 * bo_))
                dve.wait_ge(s["o_norm"], count(4 * bo_ + qo))
                num = ps.rearrange("p (t j c) -> p t j c", t=TT, j=4)
                dve.reciprocal(rden[:], num[:, :, :, HD:HD + 1]).then_inc(s["o_rec"], 1)
                dve.wait_ge(s["o_rec"], count(4 * bo_ + qo + 1))
                dve.tensor_tensor(ctxo[:, :, 64 * qo:64 * qo + 64].rearrange("p t (j d) -> p t j d", d=HD),
                                  num[:, :, :, 0:HD], rden[:].broadcast_to([P, TT, 4, HD]), ALU.mult
                                  ).then_inc(s["o_norm"], 1)
            elif name in ROUTE_FROM:
                route(name, ps, b - 1)
            elif name[0] == "W":
                h = int(name[1])
                dve.wait_ge(s["wo_mm"], count(2 * (b - 1) + h + 1))
                dve.wait_ge(s["xres_bias"], count(4 * (b - 1) + 4))
                x2 = x1[:, 2 * h:2 * h + 2, :]
                dve.tensor_tensor(x2, ps.rearrange("p (t d) -> p t d", t=2), x2, ALU.add).then_inc(s["x1_ready"], 1)

        def route(name, ps, bb):
            done = ROUTE_FROM[name]

            def then(ins):
                nonlocal done
                done += 1
                ins.then_inc(s["rt_step"], 1)
                dve.wait_ge(s["rt_step"], count(RT_ALL * bb + done))

            def wide(v):
                return v.unsqueeze(2).broadcast_to([P, TT, E])

            ranks = rank[:].unsqueeze(1).broadcast_to([P, TT, E])
            big, total, inverse, where, p1, p2, both, scale = (small[:, i, :] for i in range(8))
            if name == "R":
                dve.wait_ge(s["r_mm"], count(bb + 1))
                dve.tensor_copy(scores[:], ps[:, 0:TT * E].rearrange("p (t e) -> p t e", e=E)).then_inc(s["r_ready"], 1)
                dve.wait_ge(s["r_ready"], count(bb + 1))
                then(dve.tensor_reduce(big, scores[:], AX, ALU.max))
                then(dve.tensor_tensor(scores[:], scores[:], wide(big), ALU.subtract))
            elif name == "RTs":
                dve.wait_ge(s["rt_exp"], count(bb + 1))
                dve.wait_ge(s["route_setup"], 8)
                then(dve.tensor_reduce(total, scores[:], AX, ALU.add))
                then(dve.reciprocal(inverse, total))
                then(dve.tensor_tensor(scores[:], scores[:], wide(inverse), ALU.mult))
            elif name in ("RT1", "RT2"):
                k = int(name[2]) - 1
                p_k, src = (p1, scores) if k == 0 else (p2, masked)
                then(dve.tensor_reduce(p_k, src[:], AX, ALU.max))
                then(dve.tensor_tensor(chosen[:, k], src[:], wide(p_k), ALU.is_equal))
                then(dve.tensor_tensor(chosen[:, k], chosen[:, k], ranks, ALU.mult))
                then(dve.tensor_reduce(where, chosen[:, k], AX, ALU.max))
                then(dve.tensor_tensor(chosen[:, k], ranks, wide(where), ALU.is_equal))
                if k == 0:
                    then(dve.scalar_tensor_tensor(out=masked[:], in0=chosen[:, 0], scalar=-2.0, in1=scores[:],
                                                  op0=ALU.mult, op1=ALU.add))
            elif name == "RTw":
                then(dve.tensor_tensor(both, p1, p2, ALU.add))
                then(dve.tensor_scalar(both, both, 1e-12, None, ALU.max))
                then(dve.reciprocal(scale, both))
                then(dve.tensor_reduce(sums[:], chosen[:, 0].rearrange("p t e -> p e t"), AX, ALU.add))
            else:
                dve.wait_ge(s["rt_mm"], count(bb + 1))
                dve.wait_ge(s["xg_stored"], count(16 * NC * bb))
                dve.wait_ge(s["meta_stored"], count(16 * NC * bb))
                then(dve.tensor_tensor(place[:], ps[:, 0:NC * E].rearrange("p (c e) -> p c e", e=E),
                                       next_slot[:].unsqueeze(1).broadcast_to([P, NC, E]), ALU.add))
                then(dve.tensor_tensor(place[:], place[:], choices[:, 0:NC, :], ALU.mult))
                then(dve.tensor_reduce(slot[:], place[:], AX, ALU.add))
                then(dve.tensor_tensor(primary[:], primary[:], sums[:], ALU.add))
                then(dve.tensor_copy(slot_u[:], slot[:]))
                for k, p_k in enumerate((p1, p2)):
                    dve.tensor_copy(meta[:, k * TT:(k + 1) * TT, 0].bitcast(U32), token[:])
                    then(dve.tensor_tensor(meta[:, k * TT:(k + 1) * TT, 1], p_k, scale, ALU.mult))
                then(dve.tensor_scalar(token[:], token[:], float(T), None, ALU.add))
                ins = dve.tensor_tensor(next_slot[:], next_slot[:], ps[:, NC * E:(NC + 1) * E], ALU.add)
                ins.then_inc(s["meta_ready"], 1)
                dve.wait_ge(s["meta_ready"], count(bb + 1))
            following = [n for n in ROUTE_FROM.values() if n > ROUTE_FROM[name]] + [RT_ALL]
            assert done == following[0], (name, done)

        each_iteration(dve, body)


def experts(nc, ctx, N, E, CAP, gate_up, down, sim, out, xg_dram, meta_dram, shared):
    ident, ones, rank, next_slot, primary = (shared[n] for n in ("ident", "ones", "rank", "next_slot", "primary"))
    F2, F = gate_up.shape[1], down.shape[2]
    G = 2 * N // P + E - 1
    THRESHOLD = 0.7

    def sb(name, shape, dt=F32):
        return ctx.enter_context(nc.sbuf_tensor(name, shape, dt))

    def sem(name):
        return ctx.enter_context(nc.semaphore(name))

    raw_up = sb("raw_up", [P, E, F2 // P, DM])
    raw_down = sb("raw_down", [P, E, DM // P, F])
    Wup = sb("Wup", [P, KC, E, F2])
    Wdown = sb("Wdown", [P, F // P, E, DM])
    simb = sb("simb", [P, E, E])
    e1 = sb("e1", [P, E])
    e2 = sb("e2", [P, E])
    e3 = sb("e3", [P, E])
    first = sb("first", [P, E])
    start = sb("start", [P, E + 1])
    shift = sb("shift", [P, E + 1])
    which = sb("which", [P, E + 1])
    step_to = sb("step_to", [P, 2, E + 1])
    one_row = sb("one_row", [P, E])
    iota_e = sb("iota_e", [P, E + 1])
    sims = sb("sims", [P, E, E])
    eq = sb("eq", [P, E, E])
    tiles_at = sb("tiles_at", [P, N // P + 1])
    full = sb("full", [P, E, N // P + 1])
    g_at = sb("g_at", [P, G])
    reached = sb("reached", [P, G, E + 1])
    product = sb("product", [P, G, E + 1])
    plan_f = sb("plan_f", [P, 2, G])
    plan = sb("plan", [P, 2, G], U32)
    pad_slot = sb("pad_slot", [P, E])
    pad_slot_u = sb("pad_slot_u", [P, E], U32)
    part_at = sb("part_at", [P, 1])
    pad_meta = sb("pad_meta", [P, 2])
    zeros = sb("zeros", [P, DM])
    scrap = sb("x_scrap", [P, 1])
    SLOTS = 8
    xt = [sb(f"xt{k}", [P, DM]) for k in range(SLOTS)]
    meta = [sb(f"metat{k}", [P, 2]) for k in range(SLOTS)]
    xgT = [sb(f"xgT{u}", [P, KC, P]) for u in range(2)]
    act_g = [sb(f"act_g{u}", [P, F]) for u in range(2)]
    h = [sb(f"h{u}", [P, F]) for u in range(2)]
    hT = [sb(f"hT{u}", [P, F // P, P]) for u in range(2)]
    y = [sb(f"y{u}", [P, DM]) for u in range(2)]

    banks = [ctx.enter_context(nc.psum_tensor(f"bank{i}", [P, 512], F32)) for i in range(8)]
    psX, psU, psH, psY = banks[0:2], banks[2:4], banks[4:6], banks[6:8]

    names = """up_loaded down_loaded sim_loaded w_tr wa_ready wd_ready made pad_ready pads_stored
    step plan_ready prim_mm prim_read
    x_tr xT_ready up_mm silu_ready h_ready h_tr hT_ready y_mm y_ready y_added zero_stored turn_taken""".split()
    names += [f"tile{k}_loaded" for k in range(SLOTS)]
    s = {n: sem("x_" + n) for n in names}

    FILLS = [("up", e, k) for e in range(E) for k in range(KC)] + [("down", e, 0) for e in range(E)]

    def turns(eng, body, skew):
        for g in range(SLOTS):
            body(g, g, 0)
        rounds = (G - 1 - SLOTS) // SLOTS
        with eng.Fori(0, rounds) as i:
            for k in range(SLOTS):
                body(SLOTS * i + (SLOTS + k), k, i + 1)
        for g in range(SLOTS * (rounds + 1), G + skew):
            body(g, g % SLOTS, g // SLOTS)

    def before_end(g, n):
        return not isinstance(g, int) or g + n < G

    def has_before(g):
        return not isinstance(g, int) or g > 0

    def tile_loaded(eng, k, j):
        eng.wait_ge(s[f"tile{k}_loaded"], count(32 * j + 32))

    block = ctx.enter_context(nc.Block())

    @block.sync
    def _(sp):
        for e in range(E):
            sp.dma_start(raw_up[:, e, :, :], gate_up[e].rearrange("(b p) d -> p b d", p=P)).then_inc(s["up_loaded"], 16)
        for e in range(E):
            sp.dma_start(raw_down[:, e, :, :], down[e].rearrange("(b p) d -> p b d", p=P)).then_inc(s["down_loaded"], 16)
        sp.dma_start(simb[:].rearrange("p i j -> p (i j)"),
                     sim.rearrange("(o i) j -> o (i j)", o=1).broadcast_to([P, E * E])).then_inc(s["sim_loaded"], 16)
        sp.wait_ge(s["pad_ready"], 1)
        sp.wait_ge(s["made"], 7)
        sp.dma_start(xg_dram[E * CAP:E * CAP + P, :], zeros[:]).then_inc(s["zero_stored"], 16)
        sp.dma_start(out[N:N + P, :], zeros[:]).then_inc(s["zero_stored"], 16)
        sp.dma_start(meta_dram[E * CAP:E * CAP + P, :], pad_meta[:]).then_inc(s["zero_stored"], 16)
        sp.wait_ge(s["zero_stored"], 48)
        sp.wait_ge(s["pads_stored"], 16 * 2 * E)
        sp.wait_ge(s["plan_ready"], 1)

        def load(g, k, j):
            if isinstance(g, int) and g >= G:
                return
            row = sp.value_load(plan[0:1, 0, g:g + 1] if isinstance(g, int) else plan[0:1, 0, bass.ds(g, 1)],
                                min_val=0, max_val=E * CAP)
            sp.wait_ge(s["y_added"], count(16 * (g - SLOTS + 1)))
            sp.dma_start(xt[k][:], xg_dram[bass.ds(row, P), :]).then_inc(s[f"tile{k}_loaded"], 16)
            sp.dma_start(meta[k][:], meta_dram[bass.ds(row, P), :]).then_inc(s[f"tile{k}_loaded"], 16)

        turns(sp, load, 0)
        sp.wait_ge(s["y_added"], 16 * G)

    @block.gpsimd
    def _(pool):
        pool.memset(zeros[:], 0.0).then_inc(s["pad_ready"], 1)
        pool.iota(pad_meta[:, 0:1].bitcast(U32), [[0, 1]], base=N, channel_multiplier=1).then_inc(s["made"], 1)
        pool.memset(pad_meta[:, 1:2], 0.0).then_inc(s["made"], 1)
        pool.iota(part_at[:], [[0, 1]], base=0, channel_multiplier=1, allow_small_or_imprecise_dtypes=True
                  ).then_inc(s["made"], 1)
        pool.iota(iota_e[:], [[1, E + 1]], base=0, channel_multiplier=0, allow_small_or_imprecise_dtypes=True
                  ).then_inc(s["made"], 1)
        pool.iota(tiles_at[:], [[P, N // P + 1]], base=0, channel_multiplier=0, allow_small_or_imprecise_dtypes=True
                  ).then_inc(s["made"], 1)
        pool.iota(g_at[:], [[1, G]], base=0, channel_multiplier=0, allow_small_or_imprecise_dtypes=True
                  ).then_inc(s["made"], 1)
        pool.memset(one_row[:], 1.0).then_inc(s["made"], 1)
        pool.wait_ge(s["made"], 7)
        pool.wait_ge(s["pad_ready"], 1)
        pool.wait_ge(s["step"], 2)
        for e in range(E):
            off = bass.IndirectOffsetOnAxis(ap=pad_slot_u[:, e:e + 1], axis=0)
            pool.indirect_dma_start(xg_dram, off, zeros[:], None).then_inc(s["pads_stored"], 16)
            off = bass.IndirectOffsetOnAxis(ap=pad_slot_u[:, e:e + 1], axis=0)
            pool.indirect_dma_start(meta_dram, off, pad_meta[:], None).then_inc(s["pads_stored"], 16)


        def add(g, slot, j):
            u = slot % 2
            pool.wait_ge(s["y_ready"], count(g + 1))
            tile_loaded(pool, slot, j)
            pool.wait_ge(s["turn_taken"], count(g))
            pool.wait_ge(s["y_added"], count(16 * g))
            pool.tensor_tensor(scrap[:], zeros[:, 0:1], zeros[:, 0:1], ALU.add).then_inc(s["turn_taken"], 1)
            pool.wait_ge(s["zero_stored"], 48)
            off = bass.IndirectOffsetOnAxis(ap=meta[slot][:, 0:1].bitcast(U32), axis=0)
            pool.indirect_dma_start(out, off, y[u][:], None, compute_op=ALU.add).then_inc(s["y_added"], 16)

        turns(pool, add, 0)
        pool.wait_ge(s["turn_taken"], G)
        pool.wait_ge(s["y_added"], 16 * G)

    def weight_copy(eng, copy, done, own):
        for n, (kind, e, k) in enumerate(FILLS):
            if n % 2 != own:
                continue
            eng.wait_ge(s["w_tr"], count(n + 1))
            if kind == "up":
                ins = copy(Wup[:, k, e, :], banks[n % 8][:])
            else:
                ins = copy(Wdown[:, :, e, :], banks[n % 8][:].rearrange("p (k d) -> p k d", k=F // P))
            ins.then_inc(s[done], 1)

    @block.scalar
    def _(act):
        weight_copy(act, lambda o, i: act.activation(o, i, ACT.Copy), "wa_ready", 0)

        def transposed_x(g, u):
            act.wait_ge(s["x_tr"], count(g + 1))
            act.wait_ge(s["up_mm"], count(g - 1))
            act.activation(xgT[u][:].rearrange("p k t -> p (k t)"), psX[u][:, 0:DM], ACT.Copy
                           ).then_inc(s["xT_ready"], 1)

        transposed_x(0, 0)

        def body(g, slot, j):
            u = slot % 2
            v = 1 - u
            if before_end(g, 0):
                act.wait_ge(s["up_mm"], count(g + 1))
                act.wait_ge(s["h_ready"], count(g - 1))
                act.activation(act_g[u][:], psU[u][:, 0:F], ACT.Silu).then_inc(s["silu_ready"], 1)
            if before_end(g, 1):
                transposed_x(g + 1, v)
            if has_before(g):
                act.wait_ge(s["y_mm"], count(g))
                act.wait_ge(s["y_added"], count(16 * g - 32))
                act.activation(y[v][:], psY[v][:, 0:DM], ACT.Copy).then_inc(s["y_ready"], 1)

        turns(act, body, 1)

    @block.vector
    def _(dve):
        done = 0

        def then(ins):
            nonlocal done
            done += 1
            ins.then_inc(s["step"], 1)
            dve.wait_ge(s["step"], count(done))

        dve.wait_ge(s["made"], 7)
        then(dve.tensor_scalar(pad_slot[:], next_slot[:], part_at[:, 0:1], None, ALU.add))
        then(dve.tensor_copy(pad_slot_u[:], pad_slot[:]))
        then(dve.scalar_tensor_tensor(out=e1[:], in0=iota_e[:, 0:E], scalar=-float(CAP), in1=next_slot[:],
                                      op0=ALU.mult, op1=ALU.add))
        then(dve.tensor_tensor(full[:], e1[:].unsqueeze(2).broadcast_to([P, E, N // P + 1]),
                               tiles_at[:].unsqueeze(1).broadcast_to([P, E, N // P + 1]), ALU.is_gt))
        then(dve.tensor_reduce(e2[:], full[:], AX, ALU.add))
        then(dve.memset(start[:, 0:1], 0.0))
        then(dve.tensor_tensor_scan(start[:, 1:E + 1], one_row[:], e2[:], 0.0, ALU.mult, ALU.add))
        dve.wait_ge(s["prim_mm"], 1)
        dve.wait_ge(s["sim_loaded"], 16)
        dve.tensor_scalar(first[:], banks[7][:, 0:E], 0.0, None, ALU.is_gt).then_inc(s["prim_read"], 1)
        dve.wait_ge(s["prim_read"], 1)
        then(dve.tensor_scalar(e1[:], first[:], 1.0, 1e30, ALU.subtract, ALU.mult))
        firsts = first[:].unsqueeze(1).broadcast_to([P, E, E])
        then(dve.tensor_tensor(sims[:], simb[:], firsts, ALU.mult))
        then(dve.tensor_tensor(sims[:], sims[:], e1[:].unsqueeze(1).broadcast_to([P, E, E]), ALU.add))
        then(dve.tensor_reduce(e2[:], sims[:], AX, ALU.max))
        then(dve.tensor_tensor(eq[:], sims[:], e2[:].unsqueeze(2).broadcast_to([P, E, E]), ALU.is_equal))
        then(dve.tensor_tensor(eq[:], eq[:], rank[:].unsqueeze(1).broadcast_to([P, E, E]), ALU.mult))
        then(dve.tensor_reduce(e3[:], eq[:], AX, ALU.max))
        then(dve.tensor_tensor(e3[:], e3[:], rank[:], ALU.subtract))
        then(dve.tensor_scalar(e2[:], e2[:], THRESHOLD, None, ALU.is_ge))
        then(dve.tensor_tensor(e3[:], e3[:], e2[:], ALU.mult))
        then(dve.tensor_scalar(e1[:], first[:], -1.0, 1.0, ALU.mult, ALU.add))
        then(dve.tensor_tensor(e3[:], e3[:], e1[:], ALU.mult))
        then(dve.tensor_tensor(which[:, 0:E], iota_e[:, 0:E], e3[:], ALU.subtract))
        then(dve.tensor_copy(which[:, E:E + 1], which[:, E - 1:E]))
        then(dve.tensor_scalar(shift[:], start[:], -float(P), None, ALU.mult))
        then(dve.scalar_tensor_tensor(out=shift[:], in0=iota_e[:], scalar=float(CAP), in1=shift[:],
                                      op0=ALU.mult, op1=ALU.add))
        for i, v in enumerate((shift, which)):
            then(dve.tensor_copy(step_to[:, i, 0:1], v[:, 0:1]))
            then(dve.tensor_tensor(step_to[:, i, 1:E + 1], v[:, 1:E + 1], v[:, 0:E], ALU.subtract))
        gs = g_at[:].unsqueeze(2).broadcast_to([P, G, E + 1])
        then(dve.tensor_tensor(reached[:], gs, start[:].unsqueeze(1).broadcast_to([P, G, E + 1]), ALU.is_ge))
        for i in range(2):
            then(dve.tensor_tensor(product[:], reached[:], step_to[:, i, :].unsqueeze(1).broadcast_to([P, G, E + 1]),
                                   ALU.mult))
            then(dve.tensor_reduce(plan_f[:, i, :], product[:], AX, ALU.add))
        then(dve.scalar_tensor_tensor(out=plan_f[:, 0, :], in0=g_at[:], scalar=float(P), in1=plan_f[:, 0, :],
                                      op0=ALU.mult, op1=ALU.add))
        then(dve.tensor_scalar(plan_f[:, 0, :], plan_f[:, 0, :], float(E * CAP), None, ALU.min))
        dve.tensor_copy(plan[:], plan_f[:]).then_inc(s["plan_ready"], 1)
        weight_copy(dve, dve.tensor_copy, "wd_ready", 1)

        def body(g, slot, j):
            u = slot % 2
            dve.wait_ge(s["silu_ready"], count(g + 1))
            tile_loaded(dve, slot, j)
            dve.wait_ge(s["h_tr"], count(g - 1))
            dve.scalar_tensor_tensor(out=h[u][:], in0=psU[u][:, F:2 * F], scalar=meta[slot][:, 1:2], in1=act_g[u][:],
                                     op0=ALU.mult, op1=ALU.mult).then_inc(s["h_ready"], 1)
            dve.wait_ge(s["h_tr"], count(g + 1))
            dve.wait_ge(s["y_mm"], count(g - 1))
            dve.tensor_copy(hT[u][:].rearrange("p k t -> p (k t)"), psH[u][:, 0:F]).then_inc(s["hT_ready"], 1)

        turns(dve, body, 0)

    @block.tensor
    def _(pe):
        pe.matmul(banks[7][:, 0:E], ones[:], primary[:], start=True, stop=True).then_inc(s["prim_mm"], 1)
        for n, (kind, e, k) in enumerate(FILLS):
            if n == 7:
                pe.wait_ge(s["prim_read"], 1)
            if n >= 8:
                pe.wait_ge(s["wa_ready" if n % 2 == 0 else "wd_ready"], count((n - 8) // 2 + 1))
            if kind == "up":
                pe.wait_ge(s["up_loaded"], 16 * E)
                for f in range(F2 // P):
                    mm = pe.transpose(banks[n % 8][:, f * P:(f + 1) * P], raw_up[:, e, f, k * P:(k + 1) * P], ident[:])
            else:
                pe.wait_ge(s["down_loaded"], 16 * E)
                for kf in range(F // P):
                    for d in range(DM // P):
                        mm = pe.transpose(banks[n % 8][:, kf * DM + d * P:kf * DM + (d + 1) * P],
                                          raw_down[:, e, d, kf * P:(kf + 1) * P], ident[:])
            mm.then_inc(s["w_tr"], 1)
        pe.wait_ge(s["wa_ready"], len(FILLS) // 2)
        pe.wait_ge(s["wd_ready"], len(FILLS) // 2)
        pe.wait_ge(s["plan_ready"], 1)

        def weights_of(g):
            return pe.value_load(plan[0:1, 1, g:g + 1] if isinstance(g, int) else plan[0:1, 1, bass.ds(g, 1)],
                                 min_val=0, max_val=E - 1)

        def transpose_x(g, slot, j):
            tile_loaded(pe, slot, j)
            pe.wait_ge(s["xT_ready"], count(g - 1))
            for k in range(KC):
                mm = pe.transpose(psX[slot % 2][:, k * P:(k + 1) * P], xt[slot][:, k * P:(k + 1) * P], ident[:])
            mm.then_inc(s["x_tr"], 1)

        transpose_x(0, 0, 0)
        expert = {}

        def body(g, slot, j):
            u = slot % 2
            v = 1 - u
            if before_end(g, 0):
                if slot == 0:
                    expert[0] = weights_of(g)
                e = expert[slot]
                pe.wait_ge(s["xT_ready"], count(g + 1))
                pe.wait_ge(s["h_ready"], count(g - 1))
                for k in range(KC):
                    mm = pe.matmul(psU[u][:], xgT[u][:, k, :], Wup[:, k, bass.ds(e, 1), :].rearrange("p o f -> p (o f)"),
                                   start=(k == 0), stop=(k == KC - 1))
                    if k == 0 and slot < SLOTS - 1 and before_end(g, 1):
                        expert[slot + 1] = weights_of(g + 1)
                mm.then_inc(s["up_mm"], 1)
            if before_end(g, 1):
                transpose_x(g + 1, (slot + 1) % SLOTS, j + (slot + 1) // SLOTS)
            if has_before(g):
                e = expert[slot - 1] if slot else weights_of(g - 1)
                pe.wait_ge(s["hT_ready"], count(g))
                pe.wait_ge(s["y_ready"], count(g - 2))
                for k in range(F // P):
                    mm = pe.matmul(psY[v][:, 0:DM], hT[v][:, k, :],
                                   Wdown[:, k, bass.ds(e, 1), :].rearrange("p o d -> p (o d)"),
                                   start=(k == 0), stop=(k == F // P - 1))
                mm.then_inc(s["y_mm"], 1)
            if before_end(g, 0):
                pe.wait_ge(s["h_ready"], count(g + 1))
                pe.wait_ge(s["hT_ready"], count(g - 1))
                for k in range(F // P):
                    mm = pe.transpose(psH[u][:, k * P:(k + 1) * P], h[u][:, k * P:(k + 1) * P], ident[:])
                mm.then_inc(s["h_tr"], 1)

        turns(pe, body, 1)


_INS = ['x', 'ctx_1024', 'mask_BxS2_bf0', 'L0_xattn_Wq', 'L0_xattn_bq', 'L0_xattn_Wk', 'L0_xattn_bk', 'L0_xattn_Wv',
        'L0_xattn_bv', 'L0_xattn_Wo', 'L0_xattn_bo', 'L0_ffn_gate_weight', 'L0_ffn_gate_up_proj',
        'L0_ffn_down_proj', 'L0_ffn_similarity_matrix']


def kernel(**inputs):
    import numpy as _np
    import concourse.bacc as _bacc
    from concourse import mybir as _mybir
    from concourse.bass_utils import run_bass_kernel_spmd as _run

    nc = _bacc.Bacc("TRN2", target_bir_lowering=False, num_devices=1)
    arrays, args = {}, []
    for name in _INS:
        a = _np.ascontiguousarray(inputs[name])
        arrays[f"in_{name}_dram"] = a
        args.append(nc.dram_tensor(f"in_{name}_dram", a.shape, _mybir.dt.from_np(a.dtype), kind="ExternalInput").ap())
    b, t, d = inputs['x'].shape
    out = nc.dram_tensor("out_dram", (b * t + P, d), F32, kind="ExternalOutput").ap()
    build(nc, *args, out)
    r = _run(nc, [arrays], core_ids=[0])
    return r.results[0]["out_dram"][:b * t].reshape(b, t, d)
```
